# Optimizing a Trainium2 kernel written in Bass

```python
import numpy as np
import jax
import jax.numpy as jnp

def _softmax(x, axis=-1):
    return jax.nn.softmax(x, axis=axis)

def _gelu(x):
    return jax.nn.gelu(x, approximate=True)

def _silu(x):
    return jax.nn.silu(x)

def _sigmoid(x):
    return jax.nn.sigmoid(x)

def _layernorm(x, axis=-1, eps=1e-05):
    m = jnp.mean(x, axis=axis, keepdims=True)
    v = jnp.var(x, axis=axis, keepdims=True)
    return (x - m) / jnp.sqrt(v + eps)

def _scatter_add(tgt, idx, src, axis=0):
    return tgt.at[idx].add(src)

def _segment_sum(src, seg, n):
    return jax.ops.segment_sum(src, seg, n)
kernel_name = 'mk_seq_preln_d1_jaxref_r8_bca259'

def setup_inputs(seed: int=0):
    np.random.seed(seed)
    _w = jnp.asarray

    def _L0_attn_setup():
        import jax, jax.numpy as jnp
        import numpy as np
        DIM = 128
        HEADS = 16
        HEAD_DIM = DIM // HEADS
        NUM_FILTERS = 4
        NUM_TAPS = 101
        RES = 64

        def _fir_fft(c, sig):
            R = sig.shape[0]
            L = R + c.shape[0] - 1
            out = jnp.fft.ifft(jnp.fft.fft(sig, n=L) * jnp.fft.fft(c, n=L)).real
            return out[:R]
        key = jax.random.key(seed)
        ks = jax.random.split(key, 5)
        B, S = (2, 256)
        x = jax.random.normal(ks[0], (B, S, DIM), dtype=jnp.float32)
        Wqkv = jax.random.normal(ks[1], (3 * DIM, DIM), dtype=jnp.float32) * DIM ** (-0.5)
        Wout = jax.random.normal(ks[2], (DIM, DIM), dtype=jnp.float32) * DIM ** (-0.5)
        Wpos = jax.random.normal(ks[3], (HEADS, NUM_FILTERS), dtype=jnp.float32) * 0.5
        coeffs = jax.random.normal(ks[4], (NUM_FILTERS, NUM_TAPS), dtype=jnp.float32) * 0.05
        return {'x': x, 'Wqkv': Wqkv, 'Wout': Wout, 'Wpos': Wpos, 'coeffs': coeffs}
    _L0_attn_in = _L0_attn_setup()

    def _L0_ffn_setup():
        import jax, jax.numpy as jnp
        import numpy as np
        BS, L, D = (4, 256, 128)
        H, E, K = (8, 16, 2)
        HD = D // H
        I = 512 // H
        key = jax.random.key(seed)
        ks = jax.random.split(key, 10)
        s = lambda k, shp, fan: jax.random.normal(k, shp, jnp.float32) / np.sqrt(fan)
        return {'x': jax.random.normal(ks[0], (BS, L, D), jnp.float32), 'Wm': s(ks[1], (D, D), D), 'bm': jnp.zeros((D,), jnp.float32), 'expert_emb': jax.random.normal(ks[2], (HD, E), jnp.float32), 'W1': s(ks[3], (E, HD, I), HD), 'b1': jnp.zeros((E, I), jnp.float32), 'W2': s(ks[4], (E, I, HD), I), 'b2': jnp.zeros((E, HD), jnp.float32), 'Wo': s(ks[5], (D, D), D), 'bo': jnp.zeros((D,), jnp.float32)}
    _L0_ffn_in = _L0_ffn_setup()
    _d = {'L0_attn_x': _L0_attn_in['x'], 'L0_attn_Wqkv': _L0_attn_in['Wqkv'], 'L0_attn_Wout': _L0_attn_in['Wout'], 'L0_attn_Wpos': _L0_attn_in['Wpos'], 'L0_attn_coeffs': _L0_attn_in['coeffs'], 'L0_ffn_Wm': _L0_ffn_in['Wm'], 'L0_ffn_bm': _L0_ffn_in['bm'], 'L0_ffn_expert_emb': _L0_ffn_in['expert_emb'], 'L0_ffn_W1': _L0_ffn_in['W1'], 'L0_ffn_b1': _L0_ffn_in['b1'], 'L0_ffn_W2': _L0_ffn_in['W2'], 'L0_ffn_b2': _L0_ffn_in['b2'], 'L0_ffn_Wo': _L0_ffn_in['Wo'], 'L0_ffn_bo': _L0_ffn_in['bo']}
    _x0 = _d['L0_attn_x']
    _d['L0_attn_x'] = jax.random.normal(jax.random.fold_in(jax.random.key(seed), 1), (4, 512, 128), dtype=_x0.dtype)
    del _x0
    return _d

def reference(L0_attn_x, L0_attn_Wqkv, L0_attn_Wout, L0_attn_Wpos, L0_attn_coeffs, L0_ffn_Wm, L0_ffn_bm, L0_ffn_expert_emb, L0_ffn_W1, L0_ffn_b1, L0_ffn_W2, L0_ffn_b2, L0_ffn_Wo, L0_ffn_bo):

    def _L0_attn_ref(x, Wqkv, Wout, Wpos, coeffs):
        import jax, jax.numpy as jnp
        import numpy as np
        DIM = 128
        HEADS = 16
        HEAD_DIM = DIM // HEADS
        NUM_FILTERS = 4
        NUM_TAPS = 101
        RES = 64

        def _fir_fft(c, sig):
            R = sig.shape[0]
            L = R + c.shape[0] - 1
            out = jnp.fft.ifft(jnp.fft.fft(sig, n=L) * jnp.fft.fft(c, n=L)).real
            return out[:R]
        B, S, D = x.shape
        scale = HEAD_DIM ** (-0.5)
        proto = jnp.linspace(0.0, 1.0, RES).astype(x.dtype)
        table = jax.vmap(_fir_fft, in_axes=(0, None))(coeffs, proto).T
        r = jnp.arange(S)
        rel = jnp.abs(r[None, :] - r[:, None]).astype(jnp.float32) / max(S - 1, 1)
        idx = jnp.clip(jnp.round(rel * (RES - 1)).astype(jnp.int32), 0, RES - 1)
        pos_feat = table[idx]
        pos_bias = jnp.einsum('ijf,hf->hij', pos_feat, Wpos)
        qkv = jnp.einsum('bsd,ed->bse', x, Wqkv)
        q, k, v = jnp.split(qkv, 3, axis=-1)
        q = q.reshape(B, S, HEADS, HEAD_DIM)
        k = k.reshape(B, S, HEADS, HEAD_DIM)
        v = v.reshape(B, S, HEADS, HEAD_DIM)
        logits = jnp.einsum('bihd,bjhd->bhij', q, k) * scale + pos_bias[None]
        attn = jax.nn.softmax(logits, axis=-1)
        out = jnp.einsum('bhij,bjhd->bihd', attn, v).reshape(B, S, D)
        return jnp.einsum('bsd,ed->bse', out, Wout)

    def _L0_ffn_ref(x, Wm, bm, expert_emb, W1, b1, W2, b2, Wo, bo):
        import jax, jax.numpy as jnp
        import numpy as np
        BS, L, D = (4, 256, 128)
        H, E, K = (8, 16, 2)
        HD = D // H
        I = 512 // H
        bs, L_, d = x.shape
        h = x @ Wm + bm
        t = h.reshape(bs * L_ * H, HD)
        logits = t @ expert_emb
        w = jax.nn.softmax(logits, axis=-1)
        topw, topi = jax.lax.top_k(w, K)
        hmid = jax.nn.gelu(jnp.einsum('td,edi->tei', t, W1) + b1, approximate=False)
        eo = jnp.einsum('tei,eio->teo', hmid, W2) + b2
        sel = jnp.take_along_axis(eo, topi[:, :, None], axis=1)
        comb = (sel * topw[:, :, None]).sum(axis=1)
        out = comb.reshape(bs, L_, d)
        return out @ Wo + bo
    x = L0_attn_x
    x = x + _L0_attn_ref(_layernorm(x, axis=-1), L0_attn_Wqkv, L0_attn_Wout, L0_attn_Wpos, L0_attn_coeffs)
    x = x + _L0_ffn_ref(_layernorm(x, axis=-1), L0_ffn_Wm, L0_ffn_bm, L0_ffn_expert_emb, L0_ffn_W1, L0_ffn_b1, L0_ffn_W2, L0_ffn_b2, L0_ffn_Wo, L0_ffn_bo)
    return x

_drawn_inputs = setup_inputs


def setup_inputs(seed=0):
    import zlib

    import numpy as np

    out = dict(_drawn_inputs(seed))
    spreads = {'L0_ffn_bm': (0.0, 0.1),
     'L0_ffn_b1': (0.0, 0.1),
     'L0_ffn_b2': (0.0, 0.1),
     'L0_ffn_bo': (0.0, 0.1)}
    factors = {'L0_attn_Wpos': 7.39, 'L0_attn_coeffs': 8.0}
    for name, (base, spread) in spreads.items():
        noise = np.random.default_rng([zlib.crc32(name.encode()), seed]).standard_normal(out[name].shape)
        drawn = base * np.exp(spread * noise) if base else spread * noise
        out[name] = jnp.asarray(drawn.astype(out[name].dtype))
    for name, factor in factors.items():
        out[name] = (out[name] * factor).astype(out[name].dtype)
    return out
```

```python
import concourse.bass as bass
from concourse import mybir
from contextlib import ExitStack

B, S, D = 4, 512, 128
H, HD = 16, 8
G, HG = 4, 4
NT = S // 128
TAPS, FILT, RES = 101, 4, 64
SW = S + 3 * 128
QR = 9 * HD
KR = 96
SH, SD, E, I = 8, 16, 16, 64
HR = 6 * SD
FR = HR + 3
NU = G * B
EPS = 1e-5


def layer_kernel(nc, x, Wqkv, Wout, Wpos, coeffs, Wm, bm, emb, W1, b1, W2, b2, Wo, bo,
                 c_fir, c_comb, c_rank, out):
    f32, bf16, f32r = mybir.dt.float32, mybir.dt.bfloat16, mybir.dt.float32r
    ACT, ALU, AX = mybir.ActivationFunctionType, mybir.AluOpType, mybir.AxisListType

    qk_dram = nc.dram_tensor("qk_parts", (2, B, H, 5, HD, S), bf16, kind="Internal").ap()
    v_dram = nc.dram_tensor("v_ext", (B, NT, 128, G, HG * 32), f32, kind="Internal").ap()
    bias_hi_dram = nc.dram_tensor("bias_hi", (H, 1024), f32, kind="Internal").ap()
    bias_lo_dram = nc.dram_tensor("bias_lo", (H, 1024), f32, kind="Internal").ap()
    o_dram = nc.dram_tensor("attn_heads", (B, NT, 128, D), f32, kind="Internal").ap()
    h_dram = nc.dram_tensor("h_parts", (B, 3, 128, S), bf16, kind="Internal").ap()

    top = ExitStack()
    with top:
        def tensors(stack):
            def sb(name, shape, dt=f32):
                return stack.enter_context(nc.sbuf_tensor(name, shape, dt))

            def pb(name, shape=(128, 512), dt=f32):
                return stack.enter_context(nc.psum_tensor(name, list(shape), dt))

            def sem(name):
                return stack.enter_context(nc.semaphore(name))
            return sb, pb, sem

        sb, _, sem = tensors(top)
        ident = sb("ident", [128, 128])
        ident_r = sb("ident_r", [128, 128], f32r)
        flip = sb("flip", [128, 128])
        ident_b = sb("ident_b", [128, 128], bf16)
        wout_t = sb("wout_t", [128, D])
        wm = sb("wm", [128, D])
        wo = sb("wo", [128, D])
        emb_bd = sb("emb_bd", [128, SH * E])
        w2_bd = sb("w2_bd", [128, E // 2, 2 * SD])
        w1_pack = sb("w1_pack", [FR, E * I], bf16)
        h_pack = sb("h_pack", [FR, SH, S], bf16)
        bm_col = sb("bm_col", [128, 1])
        b2_col = sb("b2_col", [128, 2])
        bo_all = sb("bo_all", [128, D])
        comb = sb("comb", [128, 2, 2 * SD])
        rank = sb("rank", [128, E])
        half_pow = sb("half_pow", [128, 16])

        env = dict(locals())
        setup_block(nc, tensors, env)
        attention_block(nc, tensors, env)
        ffn_block(nc, tensors, env)


def setup_block(nc, tensors, v):
    f32, bf16, f32r = mybir.dt.float32, mybir.dt.bfloat16, mybir.dt.float32r
    ACT, ALU = mybir.ActivationFunctionType, mybir.AluOpType
    ident, ident_r, ident_b, flip = (v[k] for k in ("ident", "ident_r", "ident_b", "flip"))
    wout_t, wm, wo = (v[k] for k in ("wout_t", "wm", "wo"))
    emb_bd, w2_bd, w1_pack, h_pack = (v[k] for k in ("emb_bd", "w2_bd", "w1_pack", "h_pack"))
    half_pow = v["half_pow"]
    NTB = B * NT
    stack = ExitStack()
    with stack:
        sb, pb, sem = tensors(stack)
        x_all = sb("x_all", [128, NTB, D])
        xn = sb("xn", [128, NTB, D])
        xn_t = sb("xn_t", [128, B, S])
        xn_back = sb("xn_back", [128, 2, S])
        w_raw = sb("w_raw", [128, 4, D])
        wqkv_t = sb("wqkv_t", [128, 3, D])
        stats = sb("stats", [128, NTB, 6])
        mv = sb("mv", [128, NTB, 2])
        veps = sb("veps", [128, NTB])
        rstd = sb("rstd", [128, NTB])
        full = sb("full", [128, 2, 2, S])
        rest = sb("rest", [128, 2, S])
        parts = sb("parts", [128, 2, B, 3, S], bf16)
        v_ext = sb("v_ext_sb", [128, NTB, H, 32])
        fir = sb("fir", [TAPS, 1024])
        co = sb("co", [FILT, TAPS])
        wp = sb("wp", [FILT, H])
        taps_h = sb("taps_h", [TAPS, H])
        bias_hi = sb("bias_hi_sb", [H, 1024], f32r)
        bias_lo = sb("bias_lo_sb", [H, 1024], f32r)
        w1_raw = sb("w1_raw", [SD + 1, E * I])
        w1_rest = sb("w1_rest", [SD + 1, E * I])
        w1_part = sb("w1_part", [SD + 1, 3, E * I], bf16)

        p_w = pb("p_w")
        p_t = [pb(f"p_t{i}") for i in range(2)]
        p_qk = [pb(f"p_qk{i}") for i in range(2)]
        p_v = pb("p_v")
        p_b = pb("p_b", (128, 1024))

        x_in = [sem(f"x_in{b}") for b in range(B)]
        w_in, bias_in, w1_in, late_in = sem("w_in"), sem("bias_in"), sem("w1_in"), sem("late_in")
        zeroed, ones_set, ident_done, consts_done = sem("zeroed"), sem("ones_set"), sem("ident_done"), sem("consts_done")
        s_dve, var_done, rstd_done, xn_done = sem("s_dve"), sem("var_done"), sem("rstd_done"), sem("xn_done")
        wt_ready, wt_copied = sem("wt_ready"), sem("wt_copied")
        xt_ready, xt_copied = sem("xt_ready"), sem("xt_copied")
        back_ready, back_copied = sem("back_ready"), sem("back_copied")
        qk_ready, qk_first, v_ready, v_copied = sem("qk_ready"), sem("qk_first"), sem("v_ready"), sem("v_copied")
        q_done, k_done, stored = sem("q_done"), sem("k_done"), sem("stored")
        taps_ready, taps_copied, bias_ready = sem("taps_ready"), sem("taps_copied"), sem("bias_ready")
        bias_hi_done, bias_split = sem("bias_hi_done"), sem("bias_split")
        w1_done, w1_packed, s_pool = sem("w1_done"), sem("w1_packed"), sem("s_pool")
        block = stack.enter_context(nc.Block())

        @block.sync
        def _(sp):
            for b in range(B):
                sp.dma_start(x_all[:, b * NT:(b + 1) * NT, :],
                             v["x"][b].rearrange("(t p) d -> p t d", p=128)).then_inc(x_in[b], 16)
                if b == 0:
                    sp.dma_start(w_raw[:, 0:3, :], v["Wqkv"].rearrange("(c p) d -> p c d", p=128)).then_inc(w_in, 16)
                    sp.dma_start(w_raw[:, 3, :], v["Wout"]).then_inc(w_in, 16)
            for b in range(B):
                for j in range(2):
                    sp.wait_ge((q_done, k_done)[j], b + 1)
                    for c in range(5 if j == 0 else 3):
                        sp.dma_start(v["qk_dram"][j, b, :, c], parts[:, j, b, c % 3, :]).then_inc(stored, 16)
                sp.wait_ge(v_copied, b + 1)
                sp.dma_start(v["v_dram"][b].rearrange("t p g c -> p t (g c)"),
                             v_ext[:, b * NT:(b + 1) * NT, :, :].rearrange("p t h c -> p t (h c)")).then_inc(stored, 16)
            sp.wait_ge(stored, 16 * 9 * B)

        @block.gpsimd
        def _(pool):
            nc.gpsimd.memset(ident[:], 0.0).then_inc(zeroed, 1)
            nc.gpsimd.memset(flip[:], 0.0).then_inc(zeroed, 1)
            pool.wait_ge(zeroed, 2)
            nc.gpsimd.affine_select(out=ident[:], in_=ident[:], compare_op=ALU.not_equal, fill=1.0, base=0,
                                    pattern=[[-1, 128]], channel_multiplier=1).then_inc(ident_done, 1)
            nc.gpsimd.affine_select(out=flip[:], in_=flip[:], compare_op=ALU.not_equal, fill=1.0, base=-127,
                                    pattern=[[1, 128]], channel_multiplier=1).then_inc(ident_done, 1)
            nc.gpsimd.memset(half_pow[:], -0.5).then_inc(s_pool, 1)
            nc.gpsimd.memset(w2_bd[:], 0.0).then_inc(s_pool, 1)
            nc.gpsimd.memset(emb_bd[:], 0.0).then_inc(s_pool, 1)
            pool.wait_ge(s_pool, 3)
            pool.wait_ge(var_done, 1)
            nc.gpsimd.tensor_tensor(rstd[:], veps[:], half_pow[:, 0:NTB], op=ALU.pow).then_inc(rstd_done, 1)
            for b in range(B):
                pool.wait_ge(qk_first, 4 * b + 4)
                if b:
                    pool.wait_ge(k_done, b)
                nc.gpsimd.tensor_tensor(rest[:, 1, :], full[:, b % 2, 1, :], parts[:, 1, b, 0, :],
                                        op=ALU.subtract).then_inc(s_pool, 1)
                pool.wait_ge(s_pool, 4 + 2 * b)
                nc.gpsimd.tensor_scalar(parts[:, 1, b, 1, :], rest[:, 1, :], 1.0, 0.0, ALU.mult, ALU.add).then_inc(s_pool, 1)
                pool.wait_ge(s_pool, 5 + 2 * b)
                nc.gpsimd.tensor_tensor(parts[:, 1, b, 2, :], rest[:, 1, :], parts[:, 1, b, 1, :],
                                        op=ALU.subtract).then_inc(k_done, 1)
            for s in range(SH):
                pool.dma_start(emb_bd[s * SD:(s + 1) * SD, s * E:(s + 1) * E], v["emb"]).then_inc(late_in, 16)
            for e in range(2):
                pool.dma_start(w2_bd[e * I:(e + 1) * I, :, e * SD:(e + 1) * SD],
                               v["W2"].rearrange("(q e) i o -> e i q o", e=2)[e]).then_inc(late_in, 16)
            pool.wait_ge(late_in, 16 * (SH + 2))

        @block.scalar
        def _(act):
            act.dma_start(co[:], v["coeffs"]).then_inc(bias_in, 16)
            act.dma_start(wp[:], v["Wpos"]).then_inc(bias_in, 16)
            act.dma_start(fir[:], v["c_fir"]).then_inc(bias_in, 16)
            act.dma_start(w1_raw[0:SD, :].rearrange("d (e i) -> d e i", e=E), v["W1"].rearrange("e d i -> d e i")).then_inc(w1_in, 16)
            act.dma_start(w1_raw[SD:SD + 1, :], v["b1"].rearrange("(a e) i -> a (e i)", a=1)).then_inc(w1_in, 16)
            act.dma_start(wm[:], v["Wm"]).then_inc(consts_done, 16)
            act.dma_start(wo[:], v["Wo"]).then_inc(consts_done, 16)
            act.dma_start(v["comb"][:].rearrange("p a c -> p (a c)"), v["c_comb"]).then_inc(consts_done, 16)
            act.dma_start(v["rank"][:], v["c_rank"]).then_inc(consts_done, 16)
            act.dma_start(v["bm_col"][:], v["bm"].rearrange("(p a) -> p a", a=1)).then_inc(consts_done, 16)
            act.dma_start(v["b2_col"][:], v["b2"]).then_inc(consts_done, 16)
            bo_rows = bass.AP(tensor=v["bo"].tensor, offset=0, ap=[[0, 128], [1, D]])
            act.dma_start(v["bo_all"][:], bo_rows).then_inc(consts_done, 16)
            act.wait_ge(wt_ready, 1)
            nc.scalar.copy(wqkv_t[:].rearrange("p c d -> p (c d)"), p_w[:, 0:3 * D]).then_inc(wt_copied, 1)
            nc.scalar.copy(wout_t[:], p_w[:, 3 * D:4 * D]).then_inc(wt_copied, 1)
            for b in range(B):
                act.wait_ge(xt_ready, b + 1)
                nc.scalar.copy(xn_t[:, b, :], p_t[b % 2][:]).then_inc(xt_copied, 1)
                act.wait_ge(back_ready, b + 1)
                if b >= 2:
                    act.wait_ge(qk_ready, 2 * (b - 2) + 1)
                nc.scalar.copy(xn_back[:, b % 2, :], p_w[:]).then_inc(back_copied, 1)
                for j in range(2):
                    act.wait_ge(qk_ready, 2 * b + j + 1)
                    if b >= 2:
                        act.wait_ge((q_done, k_done)[j], b - 1)
                    scale = HD ** -0.5 if j == 0 else 1.0
                    nc.scalar.mul(full[:, b % 2, j, :], p_qk[j][:], scale).then_inc(qk_first, 1)
                    nc.scalar.mul(parts[:, j, b, 0, :], p_qk[j][:], scale).then_inc(qk_first, 1)
            act.wait_ge(w1_done, 1)
            for c, part in enumerate((0, 1, 2, 0, 1, 0)):
                act.dma_start(w1_pack[c * SD:(c + 1) * SD, :], w1_part[0:SD, part, :]).then_inc(w1_packed, 16)
            for part in range(3):
                act.dma_start(w1_pack[HR + part:HR + part + 1, :], w1_part[SD:SD + 1, part, :]).then_inc(w1_packed, 16)
            act.wait_ge(w1_packed, 16 * 9)
            act.wait_ge(bias_split, 1)
            act.dma_start(v["bias_hi_dram"], bias_hi[:].bitcast(f32)).then_inc(bias_in, 16)
            act.dma_start(v["bias_lo_dram"], bias_lo[:].bitcast(f32)).then_inc(bias_in, 16)
            act.wait_ge(bias_in, 16 * 5)
            act.wait_ge(consts_done, 16 * 7)

        @block.vector
        def _(dve):
            steps = [0]

            def then(ins):
                steps[0] += 1
                ins.then_inc(s_dve, 1)
                dve.wait_ge(s_dve, steps[0])

            nc.vector.memset(v_ext[:], 0.0).then_inc(ones_set, 1)
            nc.vector.memset(h_pack[HR:FR, :, :], 1.0).then_inc(ones_set, 1)
            dve.wait_ge(ones_set, 2)
            nc.vector.memset(v_ext[:, :, :, HD:HD + 1], 1.0).then_inc(ones_set, 1)
            dve.wait_ge(ident_done, 2)
            nc.vector.tensor_copy(ident_r[:], ident[:]).then_inc(ones_set, 1)
            nc.vector.tensor_copy(ident_b[:], ident[:]).then_inc(ones_set, 1)
            for b in range(B):
                dve.wait_ge(x_in[b], 16)
                for t in range(b * NT, (b + 1) * NT):
                    last = nc.vector.bn_stats(stats[:, t, :], x_all[:, t, :])
            then(last)
            for t in range(NTB):
                last = nc.vector.bn_aggr(mv[:, t, :], stats[:, t, :])
            then(last)
            nc.vector.tensor_scalar(veps[:], mv[:, :, 1], EPS, None, ALU.add).then_inc(var_done, 1)
            dve.wait_ge(rstd_done, 1)
            for t in range(NTB):
                nc.vector.tensor_scalar(xn[:, t, :], x_all[:, t, :], mv[:, t, 0:1], rstd[:, t:t + 1],
                                        ALU.subtract, ALU.mult).then_inc(xn_done, 1)
            dve.wait_ge(taps_ready, 1)
            nc.vector.tensor_copy(taps_h[:], p_b[0:TAPS, 0:H]).then_inc(taps_copied, 1)
            for b in range(B):
                dve.wait_ge(qk_first, 4 * b + 2)
                then(nc.vector.tensor_tensor(rest[:, 0, :], full[:, b % 2, 0, :], parts[:, 0, b, 0, :], op=ALU.subtract))
                then(nc.vector.tensor_copy(parts[:, 0, b, 1, :], rest[:, 0, :]))
                nc.vector.tensor_tensor(parts[:, 0, b, 2, :], rest[:, 0, :], parts[:, 0, b, 1, :],
                                        op=ALU.subtract).then_inc(q_done, 1)
                dve.wait_ge(q_done, b + 1)
                dve.wait_ge(v_ready, b + 1)
                nc.vector.tensor_copy(v_ext[:, b * NT:(b + 1) * NT, :, 0:HD],
                                      p_v[:].rearrange("p (t h d) -> p t h d", t=NT, h=H)).then_inc(v_copied, 1)
                if b == 0:
                    dve.wait_ge(bias_ready, 1)
                    then(nc.vector.tensor_copy(bias_hi[:], p_b[0:H, :]))
                    nc.vector.tensor_tensor(bias_lo[:], p_b[0:H, :], bias_hi[:].bitcast(f32),
                                            op=ALU.subtract).then_inc(bias_split, 1)
            dve.wait_ge(w1_in, 32)
            then(nc.vector.tensor_copy(w1_part[:, 0, :], w1_raw[:]))
            then(nc.vector.tensor_tensor(w1_rest[:], w1_raw[:], w1_part[:, 0, :], op=ALU.subtract))
            then(nc.vector.tensor_copy(w1_part[:, 1, :], w1_rest[:]))
            nc.vector.tensor_tensor(w1_part[:, 2, :], w1_rest[:], w1_part[:, 1, :], op=ALU.subtract).then_inc(w1_done, 1)

        @block.tensor
        def _(pe):
            pe.wait_ge(ident_done, 2)
            pe.wait_ge(bias_in, 48)
            nc.tensor.matmul(p_b[0:TAPS, 0:H], co[:], wp[:], start=True, stop=True).then_inc(taps_ready, 1)
            pe.wait_ge(w_in, 32)
            for c in range(4):
                last = nc.tensor.transpose(p_w[:, c * D:(c + 1) * D], w_raw[:, c, :], ident[:])
            last.then_inc(wt_ready, 1)
            for b in range(B):
                for t in range(NT):
                    pe.wait_ge(xn_done, b * NT + t + 1)
                    if b >= 2 and t == 0:
                        pe.wait_ge(xt_copied, b - 1)
                    last = nc.tensor.transpose(p_t[b % 2][:, t * 128:(t + 1) * 128], xn[:, b * NT + t, :], ident[:])
                last.then_inc(xt_ready, 1)
                pe.wait_ge(wt_copied, 2)
                if b:
                    pe.wait_ge(back_copied, b)
                for t in range(NT):
                    last = nc.tensor.transpose(p_w[:, t * 128:(t + 1) * 128], xn[:, b * NT + NT - 1 - t, :], flip[:])
                last.then_inc(back_ready, 1)
                pe.wait_ge(xt_copied, b + 1)
                pe.wait_ge(back_copied, b + 1)
                for j in range(2):
                    if b:
                        pe.wait_ge(qk_first, 4 * (b - 1) + 2 * j + 2)
                    tokens = xn_back[:, b % 2, :] if j == 0 else xn_t[:, b, :]
                    nc.tensor.matmul(p_qk[j][:], wqkv_t[:, j, :], tokens, start=True, stop=True).then_inc(qk_ready, 1)
                if b:
                    pe.wait_ge(v_copied, b)
                for t in range(NT):
                    last = nc.tensor.matmul(p_v[:, t * 128:(t + 1) * 128], xn_t[:, b, t * 128:(t + 1) * 128],
                                            wqkv_t[:, 2, :], start=True, stop=True)
                last.then_inc(v_ready, 1)
                if b == 0:
                    pe.wait_ge(taps_copied, 1)
                    for c in range(2):
                        last = nc.tensor.matmul(p_b[0:H, c * 512:(c + 1) * 512], taps_h[:],
                                                fir[:, c * 512:(c + 1) * 512], start=True, stop=True)
                    last.then_inc(bias_ready, 1)


def load_strip(eng, dst, dram, head, done):
    row = dram[bass.ds(head, 1), :]
    eng.dma_start(dst, bass.AP(tensor=row.tensor, offset=row.offset, ap=[[1, 128], [1, SW]])).then_inc(done, 16)


def attention_block(nc, tensors, v):
    f32, bf16, f32r = mybir.dt.float32, mybir.dt.bfloat16, mybir.dt.float32r
    ACT, ALU = mybir.ActivationFunctionType, mybir.AluOpType
    ident, ident_r, ident_b = v["ident"], v["ident_r"], v["ident_b"]
    stack = ExitStack()
    with stack:
        sb, pb, sem = tensors(stack)
        q_pack = [sb(f"q_pack{i}", [KR, HG, S], bf16) for i in range(2)]
        k_pack = [sb(f"k_pack{i}", [KR, HG, S], bf16) for i in range(2)]
        strip_max = sb("strip_max", [128, HG, SW])
        strip_hi = sb("strip_hi", [128, HG, SW], f32r)
        strip_lo = sb("strip_lo", [128, HG, SW], f32r)
        vals = [sb(f"vals{i}", [128, NT, HG * 32]) for i in range(2)]
        probs = [sb(f"probs{i}", [128, HG, NT, S]) for i in range(2)]
        dump = sb("dump", [128, 2, S], bf16)
        rowmax = [sb(f"rowmax{i}", [128, HG * NT]) for i in range(2)]
        neg_parts = [sb(f"neg_parts{i}", [128, 2, HG * NT], bf16) for i in range(2)]
        neg_rows = [sb(f"neg_rows{i}", [2 * HG * NT, 128], bf16) for i in range(2)]
        head_t = [sb(f"head_t{i}", [128, S]) for i in range(2)]
        rden = sb("rden", [128, NT, HG])
        head_o = [sb(f"head_o{i}", [128, NT, HG, HD]) for i in range(2)]

        p_s = [pb(f"p_s{i}") for i in range(2)]
        p_e = [pb(f"p_e{i}", (128, 1024)) for i in range(2)]
        p_o = pb("p_o")
        p_m = pb("p_m", (128, 1024), bf16)
        p_m32 = p_m[:].bitcast(f32)

        packs_set = sem("packs_set")
        qk_in = [[sem(f"qk_in{i}_{h}") for h in range(HG)] for i in range(2)]
        max_rows_in = [sem(f"max_rows_in{i}") for i in range(2)]
        strip_max_in = [sem(f"strip_max_in{h}") for h in range(HG)]
        strip_in = [sem(f"strip_in{h}") for h in range(HG)]
        vals_in = [sem(f"vals_in{i}") for i in range(2)]
        s_ready, s_max, neg_hi, neg_done = sem("s_ready"), sem("s_max"), sem("neg_hi"), sem("neg_done")
        neg_t, neg_copied = sem("neg_t"), sem("neg_copied")
        e_ready, e_done = sem("e_ready"), sem("e_done")
        o_ready, o_copied, o_t, o_rden, o_norm = sem("o_ready"), sem("o_copied"), sem("o_t"), sem("o_rden"), sem("o_norm")
        o_stored = [sem(f"o_stored{i}") for i in range(2)]
        block = stack.enter_context(nc.Block())

        first = lambda n: isinstance(n, int) and n < 2
        last_ = lambda n: isinstance(n, int) and n >= NU

        @block.sync
        def _(sp):
            def step(n, i, par):
                if not last_(n):
                    sp.wait_ge(neg_copied, n + 1)
                    for c in range(2):
                        sp.dma_start(q_pack[par][QR + c:QR + c + 1, :, :].rearrange("a h (t s) -> a (h t) s", t=NT),
                                     neg_rows[par][c * 16:(c + 1) * 16, :]).then_inc(max_rows_in[par], 16)
                if not (isinstance(n, int) and n < 3):
                    store(n - 3, 1 - par)

            def store(n, par):
                sp.wait_ge(o_norm, n + 1)
                sp.dma_start(v["o_dram"][bass.ds(n % B, 1), :, :, bass.ds((n // B) * HG * HD, HG * HD)]
                             .rearrange("a t p c -> p (a t) c"),
                             head_o[par][:].rearrange("p t h d -> p t (h d)")).then_inc(o_stored[par], 16)
            step(0, 0, 0)
            step(1, 0, 1)
            step(2, 1, 0)
            step(3, 1, 1)
            with sp.Fori(2, NU // 2) as i:
                step(2 * i, i, 0)
                step(2 * i + 1, i, 1)
            step(NU, NU // 2, 0)
            step(NU + 1, NU // 2, 1)
            store(NU - 1, 1)
            sp.wait_ge(o_stored[0], 16 * NU // 2)
            sp.wait_ge(o_stored[1], 16 * NU // 2)

        @block.gpsimd
        def _(pool):
            for i in range(2):
                nc.gpsimd.memset(q_pack[i][:], 0.0).then_inc(packs_set, 1)
                nc.gpsimd.memset(k_pack[i][:], 1.0).then_inc(packs_set, 1)
            pool.wait_ge(packs_set, 4)

            def load_qk(n, par, h):
                b, head = n % B, (n // B) * HG + h
                for j, dst in enumerate((q_pack[par], k_pack[par])):
                    row = v["qk_dram"][j, bass.ds(b, 1), bass.ds(head, 1), 0:3, :, :].rearrange("a h c d t -> (a h c d) t")
                    src = row.unsqueeze(0).broadcast_to([3, 3 * HD, S])
                    if j == 0:
                        src = bass.AP(tensor=src.tensor, offset=src.offset, ap=[[HD * S, 3], [S, 3 * HD], [1, S]])
                    pool.dma_start(dst[0:QR, h, :], src).then_inc(qk_in[par][h], 16)

            def load_vals(n, par):
                pool.dma_start(vals[par][:], v["v_dram"][bass.ds(n % B, 1), :, :, bass.ds(n // B, 1), :]
                               .rearrange("a t p g c -> p (a t) (g c)")).then_inc(vals_in[par], 16)

            for h in range(HG):
                load_qk(0, 0, h)
                load_strip(pool, strip_max[:, h, :], v["bias_hi_dram"], h, strip_max_in[h])
            for h in range(HG):
                load_qk(1, 1, h)
            for h in range(HG):
                load_strip(pool, strip_hi[:, h, :].bitcast(f32), v["bias_hi_dram"], h, strip_in[h])
                load_strip(pool, strip_lo[:, h, :].bitcast(f32), v["bias_lo_dram"], h, strip_in[h])
            load_vals(0, 0)
            load_vals(1, 1)

            def step(n, par, strips_max, strips, more):
                for h in range(HG):
                    if strips is not None:
                        pool.wait_ge(e_ready, 2 * ((n - 1) * HG + h) + 2)
                        load_strip(pool, strip_hi[:, h, :].bitcast(f32), v["bias_hi_dram"], strips * HG + h, strip_in[h])
                        load_strip(pool, strip_lo[:, h, :].bitcast(f32), v["bias_lo_dram"], strips * HG + h, strip_in[h])
                    if more is not None:
                        pool.wait_ge(e_ready, 2 * ((n - 1) * HG + h) + 2)
                        load_qk(n + 1, 1 - par, h)
                    if strips_max is not None:
                        pool.wait_ge(s_max, (n * HG + h + 1) * NT)
                        load_strip(pool, strip_max[:, h, :], v["bias_hi_dram"], strips_max * HG + h, strip_max_in[h])

            def vals_step(n, par):
                pool.wait_ge(o_ready, n - 1)
                load_vals(n, par)

            step(1, 1, None, None, 1)
            step(2, 0, None, None, 1)
            vals_step(2, 0)
            step(3, 1, 1, None, 1)
            vals_step(3, 1)
            with pool.Fori(1, G - 1) as g:
                for c in range(B):
                    n = g * B + c
                    step(n, c % 2, g + 1 if c == 3 else None, g if c == 0 else None, 1)
                    vals_step(n, c % 2)
            for c in range(B):
                n = (G - 1) * B + c
                step(n, c % 2, None, G - 1 if c == 0 else None, 1 if n + 1 < NU else None)
                vals_step(n, c % 2)

        @block.scalar
        def _(act):
            def step(n, i, par):
                if not (isinstance(n, int) and (n == 0 or n > NU)):
                    for h in range(HG):
                        for k in range(2):
                            t = 2 * ((n - 1) * HG + h) + k
                            if h == 0 and k == 0 and not (isinstance(n, int) and n < 3):
                                act.wait_ge(o_ready, n - 2)
                            act.wait_ge(e_ready, t + 1)
                            nc.scalar.activation(probs[1 - par][:, h, 2 * k:2 * k + 2, :].rearrange("p a s -> p (a s)"),
                                                 p_e[k][:], ACT.Exp).then_inc(e_done, 1)
                if not first(n):
                    act.wait_ge(o_ready, n - 1)
                    if not (isinstance(n, int) and n < 4):
                        act.wait_ge(o_t, n - 3)
                    nc.scalar.copy(head_t[par][:], p_o[:]).then_inc(o_copied, 1)
            step(0, 0, 0)
            step(1, 0, 1)
            step(2, 1, 0)
            step(3, 1, 1)
            with act.Fori(2, NU // 2) as i:
                step(2 * i, i, 0)
                step(2 * i + 1, i, 1)
            step(NU, NU // 2, 0)
            step(NU + 1, NU // 2, 1)

        @block.vector
        def _(dve):
            scores = dve.alloc_register("scores_waited")
            dve.reg_mov(scores, 1)

            def norm(n, par):
                dve.wait_ge(o_t, n + 1)
                heads = p_m32.rearrange("p (t h c) -> p t h c", t=NT, h=HG)
                if not (isinstance(n, int) and n < 1):
                    dve.wait_ge(o_norm, n)
                nc.vector.reciprocal(rden[:], heads[:, :, :, HD]).then_inc(o_rden, 1)
                dve.wait_ge(o_rden, n + 1)
                if not (isinstance(n, int) and n < 2):
                    dve.wait_ge(o_stored[par], 16 * (n // 2))
                nc.vector.tensor_tensor(head_o[par][:], heads[:, :, :, 0:HD],
                                        rden[:].unsqueeze(3).broadcast_to([128, NT, HG, HD]),
                                        op=ALU.mult).then_inc(o_norm, 1)

            def step(n, i, par):
                if not last_(n):
                    for h in range(HG):
                        if h == 1 and not (isinstance(n, int) and n < 3):
                            norm(n - 3, 1 - par)
                        dve.wait_ge(strip_max_in[h], 16 * (n // B + 1))
                        if h == 0 and not first(n):
                            dve.wait_ge(neg_done, n - 1)
                        for t in range(NT):
                            dve.wait_ge(s_ready, scores)
                            dve.reg_add(scores, scores, 1)
                            nc.vector.tensor_tensor_reduce(
                                out=dump[:, t % 2, :], in0=p_s[t % 2][:], in1=strip_max[:, h, t * 128:t * 128 + S],
                                scale=1.0, scalar=-3.0e38, op0=ALU.add, op1=ALU.max,
                                accum_out=rowmax[par][:, h * NT + t:h * NT + t + 1]).then_inc(s_max, 1)
                    dve.wait_ge(s_max, (n + 1) * HG * NT)
                    if not first(n):
                        dve.wait_ge(neg_t, n - 1)
                    nc.vector.tensor_scalar(neg_parts[par][:, 0, :], rowmax[par][:], -1.0, None, ALU.mult).then_inc(neg_hi, 1)
                    dve.wait_ge(neg_hi, n + 1)
                    nc.vector.scalar_tensor_tensor(out=neg_parts[par][:, 1, :], in0=rowmax[par][:], scalar=-1.0,
                                                   in1=neg_parts[par][:, 0, :], op0=ALU.mult, op1=ALU.subtract).then_inc(neg_done, 1)
                    dve.wait_ge(neg_t, n + 1)
                    if not first(n):
                        dve.wait_ge(max_rows_in[par], 32 * (n // 2))
                    nc.vector.tensor_copy(neg_rows[par][:], p_m[0:32, 0:128]).then_inc(neg_copied, 1)
                elif n == NU:
                    norm(n - 3, 1 - par)
                elif n == NU + 1:
                    norm(n - 3, 1 - par)
                    norm(n - 2, par)
            for n in range(6):
                step(n, n // 2, n % 2)
            with dve.Fori(3, NU // 2) as i:
                step(2 * i, i, 0)
                step(2 * i + 1, i, 1)
            step(NU, NU // 2, 0)
            step(NU + 1, NU // 2, 1)

        @block.tensor
        def _(pe):
            def rows_of_queries(n, par, h, t):
                a = (n * HG + h) * NT + t
                if t == 0:
                    pe.wait_ge(qk_in[par][h], 32 * (n // 2 + 1))
                if not (isinstance(n, int) and n == 0 and h == 0 and t < 2):
                    pe.wait_ge(s_max, a - 1)
                nc.tensor.matmul(p_s[t % 2][:], q_pack[par][0:QR, h, t * 128:(t + 1) * 128],
                                 k_pack[par][0:QR, h, :], start=True, stop=True).then_inc(s_ready, 1)

            def rows_of_keys(n, par, h, t):
                e = 2 * (n * HG + h) + t // 2
                if h == 0 and t == 0:
                    pe.wait_ge(max_rows_in[par], 32 * (n // 2 + 1))
                if t == 0:
                    pe.wait_ge(strip_in[h], 32 * (n // B + 1))
                if t % 2 == 0 and not (isinstance(n, int) and n == 0 and h == 0):
                    pe.wait_ge(e_done, e - 1)
                dst = p_e[t // 2][:, (t % 2) * 512:(t % 2 + 1) * 512]
                w = t * 128
                nc.tensor.matmul(dst, k_pack[par][:, h, t * 128:(t + 1) * 128], q_pack[par][:, h, :], start=True, stop=False)
                nc.tensor.matmul(dst, ident_r[:], strip_hi[:, h, w:w + S], start=False, stop=False)
                last = nc.tensor.matmul(dst, ident_r[:], strip_lo[:, h, w:w + S], start=False, stop=True)
                if t % 2:
                    last.then_inc(e_ready, 1)

            def values(n, par, t):
                if t == 0:
                    pe.wait_ge(e_done, 2 * HG * (n + 1))
                    pe.wait_ge(vals_in[par], 16 * (n // 2 + 1))
                    if not (isinstance(n, int) and n == 0):
                        pe.wait_ge(o_copied, n)
                for h in range(HG):
                    last = nc.tensor.matmul(p_o[32 * h:32 * h + 32, :], vals[par][:, t, 32 * h:32 * h + 32],
                                            probs[par][:, h, t, :], start=t == 0, stop=t == NT - 1)
                if t == NT - 1:
                    last.then_inc(o_ready, 1)

            def outputs_t(n, par):
                pe.wait_ge(o_copied, n + 1)
                for t in range(NT):
                    last = nc.tensor.transpose(p_m32[:, t * 128:(t + 1) * 128], head_t[par][:, t * 128:(t + 1) * 128], ident[:])
                last.then_inc(o_t, 1)

            def step(n, i, par):
                a, last_a = 0, 0
                for s in range(HG * NT):
                    h, t = s // NT, s % NT
                    if not last_(n):
                        upto = min(16, ((s + 1) * 3 + 1) // 2)
                        while a < upto:
                            rows_of_queries(n, par, a // NT, a % NT)
                            a += 1
                    if s == 2 and not (isinstance(n, int) and n < 3):
                        if isinstance(n, int) and n > NU:
                            pe.wait_ge(o_norm, n - 3)
                        else:
                            pe.wait_ge(neg_copied, n)
                        outputs_t(n - 3, 1 - par)
                    if s == 13 and not last_(n):
                        pe.wait_ge(neg_done, n + 1)
                        if not (isinstance(n, int) and n < 3):
                            pe.wait_ge(o_norm, n - 2)
                        elif n > 0:
                            pe.wait_ge(neg_copied, n)
                        nc.tensor.transpose(p_m[0:32, 0:128], neg_parts[par][:].rearrange("p a c -> p (a c)"), ident_b[:]).then_inc(neg_t, 1)
                    if not (isinstance(n, int) and (n == 0 or n > NU)):
                        rows_of_keys(n - 1, 1 - par, h, t)
                    if t == NT - 1 and not first(n):
                        values(n - 2, par, h)
                if isinstance(n, int) and n == NU + 1:
                    pe.wait_ge(o_norm, n - 2)
                    outputs_t(n - 2, par)
            pe.wait_ge(packs_set, 4)
            step(0, 0, 0)
            step(1, 0, 1)
            step(2, 1, 0)
            step(3, 1, 1)
            with pe.Fori(2, NU // 2) as i:
                step(2 * i, i, 0)
                step(2 * i + 1, i, 1)
            step(NU, NU // 2, 0)
            step(NU + 1, NU // 2, 1)


def ffn_block(nc, tensors, v):
    f32, bf16, f32r = mybir.dt.float32, mybir.dt.bfloat16, mybir.dt.float32r
    ACT, ALU, AX = mybir.ActivationFunctionType, mybir.AluOpType, mybir.AxisListType
    ident, ident_r, comb, rank = v["ident"], v["ident_r"], v["comb"], v["rank"]
    wout_t, wm, wo, emb_bd, w2_bd = v["wout_t"], v["wm"], v["wo"], v["emb_bd"], v["w2_bd"]
    w1_pack, h_pack = v["w1_pack"], v["h_pack"]
    EP = E // 2
    UNITS = SH // 2 * EP
    GRP = SH // 2 * 2
    GT = NT * SH
    stack = ExitStack()
    with stack:
        sb, pb, sem = tensors(stack)
        x_t = sb("x_t", [128, NT, D])
        o_t = sb("o_t", [128, NT, D])
        on_t = sb("on_t", [128, S])
        x1 = sb("x1", [128, NT, D])
        x1_bo = sb("x1_bo", [128, 2 * S])
        stats = sb("stats2", [128, NT, 6])
        mv = sb("mv2", [128, NT, 2])
        veps = sb("veps2", [128, NT])
        rstd = sb("rstd2", [128, NT])
        xn2 = sb("xn2", [128, NT, D])
        xn2_t = sb("xn2_t", [128, S])
        h_t = sb("h_t", [128, S])
        h_rest = sb("h_rest", [128, S])
        h_part = sb("h_part", [128, 3, S], bf16)
        lg, key, top1, top2, ex = (sb(k, [128, GT, E]) for k in ("lg", "key", "top1", "top2", "ex"))
        best, denom = sb("best", [128, GT]), sb("denom", [128, GT])
        wt_hi = sb("wt_hi", [128, 2 * S], f32r)
        wt_lo = sb("wt_lo", [128, 2 * S], f32r)
        hid = sb("hid", [128, 8, 2, S])
        w_rows = sb("w_rows", [128, 2, S])
        weighted = sb("weighted", [128, SH, 2, S])
        c_t = sb("c_t", [128, S])
        out_sb = sb("out_sb", [128, NT, D])
        picks = sb("picks", [128, SH * E * SD], f32r)
        picks_done = sem("picks_done")
        p_g = [pb(f"p_g{i}", (128, 1024)) for i in range(2)]
        p_y = [pb(f"p_y{i}") for i in range(2)]
        p_x, p_f = pb("p_x"), pb("p_f")
        p_c = p_y[1]

        x_in, o_in = sem("x2_in"), sem("o_in")
        h_in = [sem(f"h_in{p}") for p in range(SH // 2)]
        h_stored, out_stored = sem("h_stored"), sem("out_stored")
        f_pe, f_act, f_dve, f_pool = sem("f_pe"), sem("f_act"), sem("f_dve"), sem("f_pool")
        x1_done, xn2_done, h_split, gate_done = sem("x1_done"), sem("xn2_done"), sem("h_split"), sem("gate_done")
        lg_done, wt_lo_done, veps_done = sem("lg_done"), sem("wt_lo_done"), sem("veps_done")
        g_ready, g_done = sem("g_ready"), sem("g_done")
        x_ready, y_ready, x_copied, m_done = sem("x_ready"), sem("y_ready"), sem("x_copied"), sem("m_done")
        c_ready, c_copied, r_ready, out_done = sem("c_ready"), sem("c_copied"), sem("r_ready"), sem("out_done")
        block = stack.enter_context(nc.Block())

        T_OT, T_PROJ, T_XT, T_H, T_GATE, T_WT = 2, 7, 11, 14, 16, 29
        T_EXP = 20

        def zero(n):
            return isinstance(n, int) and n == 0

        @block.sync
        def _(sp):
            def load_tokens(n):
                sp.dma_start(x_t[:], v["x"][bass.ds(n, 1)].rearrange("a (t p) d -> p (a t) d", p=128)).then_inc(x_in, 16)
                sp.dma_start(o_t[:], v["o_dram"][bass.ds(n, 1)].rearrange("a t p d -> p (a t) d")).then_inc(o_in, 16)

            def front(n, more):
                sp.wait_ge(h_split, n + 1)
                sp.dma_start(v["h_dram"][bass.ds(n, 1)].rearrange("a c p t -> p (a c) t"), h_part[:]).then_inc(h_stored, 16)
                if more:
                    load_tokens(n + 1)
                sp.wait_ge(h_stored, 16 * (n + 1))
                for p in range(SH // 2):
                    if not zero(n):
                        sp.wait_ge(g_ready, (n - 1) * UNITS + (p + 1) * EP)
                    row = 0
                    for part, reps in enumerate((3, 2, 1)):
                        for s in range(2 * p, 2 * p + 2):
                            src = v["h_dram"][bass.ds(n, 1), part, s * SD:(s + 1) * SD, :].rearrange("z d t -> (z d) t")
                            sp.dma_start(h_pack[row:row + reps * SD, s, :],
                                         src.unsqueeze(0).broadcast_to([reps, SD, S])).then_inc(h_in[p], 16)
                        row += reps * SD

            def result(b):
                sp.wait_ge(out_done, b + 1)
                sp.dma_start(v["out"][bass.ds(b, 1)].rearrange("a (t p) d -> p (a t) d", p=128), out_sb[:]).then_inc(out_stored, 16)

            load_tokens(0)
            front(0, True)
            with sp.Fori(0, B - 2) as b:
                front(b + 1, True)
                result(b)
            front(B - 1, False)
            result(B - 2)
            result(B - 1)
            sp.wait_ge(out_stored, 16 * B)

        @block.gpsimd
        def _(pool):
            with pool.Fori(0, B) as b:
                pool.wait_ge(veps_done, b + 1)
                nc.gpsimd.tensor_tensor(rstd[:], veps[:], v["half_pow"][:, 0:NT], op=ALU.pow).then_inc(f_pool, 1)

        @block.scalar
        def _(act):
            def front(u, n):
                if u == T_OT:
                    act.wait_ge(f_pe, 6 * n + 1)
                    nc.scalar.copy(on_t[:], p_f[:]).then_inc(f_act, 1)
                if u == T_XT:
                    act.wait_ge(f_pe, 6 * n + 3)
                    nc.scalar.copy(xn2_t[:], p_f[:]).then_inc(f_act, 1)
                if u == T_H:
                    act.wait_ge(f_pe, 6 * n + 4)
                    if not zero(n):
                        act.wait_ge(h_split, n)
                    nc.scalar.activation(h_t[:], p_f[:], ACT.Identity, bias=v["bm_col"][:]).then_inc(f_act, 1)
                if u == T_EXP:
                    act.wait_ge(lg_done, n + 1)
                    nc.scalar.activation(ex[:].rearrange("p a e -> p (a e)"), lg[:].rearrange("p a e -> p (a e)"),
                                         ACT.Exp).then_inc(f_act, 1)
                if u == T_WT:
                    act.wait_ge(f_pe, 6 * n + 6)
                    nc.scalar.copy(wt_hi[:, bass.ds((n % 2) * S, S)], p_f[:]).then_inc(f_act, 1)

            def x_copy(b, k):
                act.wait_ge(x_ready, 2 * GRP * b + k + 1)
                if not (zero(b) and k < 2):
                    act.wait_ge(m_done, 2 * GRP * b + k - 1)
                nc.scalar.copy(w_rows[:, k % 2, :], p_x[:]).then_inc(x_copied, 1)

            def last_copies(b, u):
                if u in (1, 3):
                    x_copy(b, 2 * GRP - 2 + u // 2)
                if u == 4:
                    act.wait_ge(c_ready, b + 1)
                    if not zero(b):
                        act.wait_ge(r_ready, b)
                    nc.scalar.copy(c_t[:], p_c[:]).then_inc(c_copied, 1)

            def experts(b, n):
                for u in range(UNITS):
                    act.wait_ge(g_ready, UNITS * b + u + 1)
                    if u % 4 == 0 and not (zero(b) and u < 8):
                        act.wait_ge(y_ready, 2 * (GRP * b + u // 4 - 1))
                    nc.scalar.activation(hid[:, u % 8, :, :].rearrange("p a s -> p (a s)"), p_g[u % 2][:],
                                         ACT.Gelu).then_inc(g_done, 1)
                    if u > 4 and u % 2 == 1 and u < UNITS:
                        x_copy(b, (u - 5) // 2)
                    if not zero(b):
                        last_copies(b - 1, u)
                    if n is not None:
                        front(u, n)

            for u in range(UNITS):
                front(u, 0)
            experts(0, 1)
            with act.Fori(1, B - 1) as b:
                experts(b, b + 1)
            experts(B - 1, None)
            for u in range(UNITS):
                last_copies(B - 1, u)

        @block.vector
        def _(dve):
            LINKS = 19
            links = [0]

            def link(ins, n):
                links[0] += 1
                ins.then_inc(f_dve, 1)
                dve.wait_ge(f_dve, LINKS * n + links[0])

            def over_e(a):
                return a[:].unsqueeze(2).broadcast_to([128, GT, E])

            def front(u, n):
                logits = p_f[:].rearrange("p (a e) -> p a e", e=E)
                ranks = rank[:].unsqueeze(1).broadcast_to([128, GT, E])
                if u == 0:
                    links[0] = 0
                if u == T_PROJ:
                    dve.wait_ge(x_in, 16 * (n + 1))
                    dve.wait_ge(f_pe, 6 * n + 2)
                    link(nc.vector.tensor_tensor(x1[:].rearrange("p t d -> p (t d)"), p_f[:],
                                                 x_t[:].rearrange("p t d -> p (t d)"), op=ALU.add), n)
                    for t in range(NT):
                        last = nc.vector.bn_stats(stats[:, t, :], x1[:, t, :])
                    link(last, n)
                    if not (isinstance(n, int) and n < 2):
                        dve.wait_ge(out_done, n - 1)
                    nc.vector.tensor_tensor(x1_bo[:, bass.ds((n % 2) * S, S)].rearrange("p (t d) -> p t d", t=NT), x1[:],
                                            v["bo_all"][:].unsqueeze(1).broadcast_to([128, NT, D]),
                                            op=ALU.add).then_inc(x1_done, 1)
                    for t in range(NT):
                        last = nc.vector.bn_aggr(mv[:, t, :], stats[:, t, :])
                    link(last, n)
                    nc.vector.tensor_scalar(veps[:], mv[:, :, 1], EPS, None, ALU.add).then_inc(veps_done, 1)
                if u == T_PROJ + 3:
                    dve.wait_ge(f_pool, n + 1)
                    for t in range(NT):
                        last = nc.vector.tensor_scalar(xn2[:, t, :], x1[:, t, :], mv[:, t, 0:1], rstd[:, t:t + 1],
                                                       ALU.subtract, ALU.mult)
                    last.then_inc(xn2_done, 1)
                if u == T_H:
                    dve.wait_ge(f_act, 5 * n + 3)
                    if not zero(n):
                        dve.wait_ge(h_stored, 16 * n)
                    link(nc.vector.tensor_copy(h_part[:, 0, :], h_t[:]), n)
                    link(nc.vector.tensor_tensor(h_rest[:], h_t[:], h_part[:, 0, :], op=ALU.subtract), n)
                    link(nc.vector.tensor_copy(h_part[:, 1, :], h_rest[:]), n)
                    nc.vector.tensor_tensor(h_part[:, 2, :], h_rest[:], h_part[:, 1, :], op=ALU.subtract).then_inc(h_split, 1)
                if u == T_GATE + 1:
                    dve.wait_ge(f_pe, 6 * n + 5)
                    link(nc.vector.tensor_reduce(best[:], logits, axis=AX.X, op=ALU.max), n)
                    nc.vector.tensor_tensor(lg[:], logits, over_e(best), op=ALU.subtract).then_inc(lg_done, 1)
                    dve.wait_ge(lg_done, n + 1)
                if u == T_GATE + 2:
                    link(nc.vector.scalar_tensor_tensor(out=key[:], in0=lg[:], scalar=0.0, in1=ranks,
                                                        op0=ALU.is_ge, op1=ALU.mult), n)
                    link(nc.vector.tensor_reduce(best[:], key[:], axis=AX.X, op=ALU.max), n)
                if u == T_GATE + 4:
                    link(nc.vector.tensor_tensor(top1[:], key[:], over_e(best), op=ALU.is_equal), n)
                    link(nc.vector.scalar_tensor_tensor(out=top2[:], in0=top1[:], scalar=-3.0e38, in1=lg[:],
                                                        op0=ALU.mult, op1=ALU.add), n)
                if u == T_GATE + 6:
                    link(nc.vector.tensor_reduce(best[:], top2[:], axis=AX.X, op=ALU.max), n)
                    link(nc.vector.tensor_tensor(key[:], top2[:], over_e(best), op=ALU.is_equal), n)
                if u == T_GATE + 7:
                    link(nc.vector.tensor_tensor(key[:], key[:], ranks, op=ALU.mult), n)
                    link(nc.vector.tensor_reduce(best[:], key[:], axis=AX.X, op=ALU.max), n)
                if u == T_GATE + 9:
                    link(nc.vector.tensor_tensor(top2[:], key[:], over_e(best), op=ALU.is_equal), n)
                    dve.wait_ge(f_act, 5 * n + 4)
                    nc.vector.tensor_reduce(denom[:], ex[:], axis=AX.X, op=ALU.add)
                    link(nc.vector.tensor_tensor(top1[:], top1[:], top2[:], op=ALU.add), n)
                if u == T_GATE + 11:
                    link(nc.vector.reciprocal(denom[:], denom[:]), n)
                    link(nc.vector.tensor_tensor(top1[:], top1[:], ex[:], op=ALU.mult), n)
                    nc.vector.tensor_tensor(lg[:], top1[:], over_e(denom), op=ALU.mult).then_inc(gate_done, 1)
                if u == T_WT:
                    dve.wait_ge(f_act, 5 * n + 5)
                    w = bass.ds((n % 2) * S, S)
                    nc.vector.tensor_tensor(wt_lo[:, w], p_f[:], wt_hi[:, w].bitcast(f32), op=ALU.subtract).then_inc(wt_lo_done, 1)
                if u == UNITS - 1:
                    assert links[0] == LINKS, links[0]

            def weigh(b, k):
                g, a = k // 2, k % 2
                pair, half = g // 2, g % 2
                dve.wait_ge(x_copied, 2 * GRP * b + k + 1)
                dve.wait_ge(y_ready, 2 * GRP * b + k + 1)
                if k == 0 and not zero(b):
                    dve.wait_ge(c_ready, b)
                nc.vector.scalar_tensor_tensor(out=weighted[:, 2 * pair + a, half, :], in0=p_y[k % 2][:],
                                               scalar=v["b2_col"][:, half:half + 1], in1=w_rows[:, k % 2, :],
                                               op0=ALU.add, op1=ALU.mult).then_inc(m_done, 1)

            def last_steps(b, u):
                if u in (1, 3):
                    weigh(b, 2 * GRP - 2 + u // 2)
                if u == 6:
                    dve.wait_ge(r_ready, b + 1)
                    if not zero(b):
                        dve.wait_ge(out_stored, 16 * b)
                    nc.vector.tensor_tensor(out_sb[:].rearrange("p t d -> p (t d)"), p_c[:],
                                            x1_bo[:, bass.ds((b % 2) * S, S)], op=ALU.add).then_inc(out_done, 1)

            def experts(b, n):
                for u in range(UNITS):
                    if u > 4 and u % 2 == 1:
                        weigh(b, (u - 5) // 2)
                    if not zero(b):
                        last_steps(b - 1, u)
                    if n is not None:
                        front(u, n)

            nc.vector.tensor_copy(picks[:].rearrange("p (a o) -> p a o", o=SD),
                                  ident[:].unsqueeze(2).broadcast_to([128, 128, SD])).then_inc(picks_done, 1)
            for u in range(UNITS):
                front(u, 0)
            experts(0, 1)
            with dve.Fori(1, B - 1) as b:
                experts(b, b + 1)
            experts(B - 1, None)
            for u in range(UNITS):
                last_steps(B - 1, u)

        @block.tensor
        def _(pe):
            def front(u, n):
                if u == T_OT:
                    pe.wait_ge(o_in, 16 * (n + 1))
                    if not zero(n):
                        pe.wait_ge(wt_lo_done, n)
                    for t in range(NT):
                        last = nc.tensor.transpose(p_f[:, t * 128:(t + 1) * 128], o_t[:, NT - 1 - t, :], v["flip"][:])
                    last.then_inc(f_pe, 1)
                if u == T_PROJ:
                    pe.wait_ge(f_act, 5 * n + 1)
                    for t in range(NT):
                        last = nc.tensor.matmul(p_f[:, t * 128:(t + 1) * 128], on_t[:, t * 128:(t + 1) * 128], wout_t[:],
                                                start=True, stop=True)
                    last.then_inc(f_pe, 1)
                if u == T_XT:
                    pe.wait_ge(xn2_done, n + 1)
                    for t in range(NT):
                        last = nc.tensor.transpose(p_f[:, t * 128:(t + 1) * 128], xn2[:, t, :], ident[:])
                    last.then_inc(f_pe, 1)
                if u == T_H:
                    pe.wait_ge(f_act, 5 * n + 2)
                    nc.tensor.matmul(p_f[:], wm[:], xn2_t[:], start=True, stop=True).then_inc(f_pe, 1)
                if u == T_GATE:
                    pe.wait_ge(f_act, 5 * n + 3)
                    for t in range(NT):
                        last = nc.tensor.matmul(p_f[:, t * 128:(t + 1) * 128], h_t[:, t * 128:(t + 1) * 128], emb_bd[:],
                                                start=True, stop=True)
                    last.then_inc(f_pe, 1)
                if u == T_WT:
                    pe.wait_ge(gate_done, n + 1)
                    w = lg[:].rearrange("p (t a) e -> p t (a e)", t=NT)
                    for t in range(NT):
                        last = nc.tensor.transpose(p_f[:, t * 128:(t + 1) * 128], w[:, t, :], ident[:])
                    last.then_inc(f_pe, 1)

            def outputs(b, k):
                g, a = k // 2, k % 2
                pair, half = g // 2, g % 2
                s = 2 * pair + a
                if not (zero(b) and k == 0):
                    pe.wait_ge(x_copied, 2 * GRP * b + k)
                if k == 0:
                    pe.wait_ge(picks_done, 1)
                    pe.wait_ge(wt_lo_done, b + 1)
                first = (s * E + half * 8) * SD
                pick = picks[:, first:first + 128]
                w = bass.ds((b % 2) * S, S)
                nc.tensor.matmul(p_x[:], pick, wt_hi[:, w], start=True, stop=False)
                nc.tensor.matmul(p_x[:], pick, wt_lo[:, w], start=False, stop=True).then_inc(x_ready, 1)
                pe.wait_ge(g_done, UNITS * b + 4 * (g + 1))
                if not (zero(b) and k < 2):
                    pe.wait_ge(m_done, 2 * GRP * b + k - 1)
                if k == 1 and not zero(b):
                    pe.wait_ge(out_done, b)
                for q in range(4):
                    last = nc.tensor.matmul(p_y[k % 2][32 * q:32 * q + 32, :], w2_bd[:, 4 * half + q, :],
                                            hid[:, 4 * (g % 2) + q, a, :], start=True, stop=True)
                last.then_inc(y_ready, 1)

            def last_products(b, u):
                if u in (1, 3):
                    outputs(b, 2 * GRP - 2 + u // 2)
                if u == 4:
                    pe.wait_ge(m_done, 2 * GRP * (b + 1))
                    for k in range(2):
                        for half in range(2):
                            for c in range(4):
                                last = nc.tensor.matmul(p_c[32 * c:32 * c + 32, :], comb[:, k, :],
                                                        weighted[:, 2 * c + k, half, :],
                                                        start=(k, half) == (0, 0), stop=(k, half) == (1, 1))
                    last.then_inc(c_ready, 1)
                if u == 5:
                    pe.wait_ge(c_copied, b + 1)
                    for t in range(NT):
                        last = nc.tensor.matmul(p_c[:, t * 128:(t + 1) * 128], c_t[:, t * 128:(t + 1) * 128], wo[:],
                                                start=True, stop=True)
                    last.then_inc(r_ready, 1)

            def experts(b, n):
                for u in range(UNITS):
                    pair, q = u // EP, u % EP
                    if q == 0:
                        pe.wait_ge(h_in[pair], 96 * (b + 1))
                    if not (zero(b) and u < 2):
                        pe.wait_ge(g_done, UNITS * b + u - 1)
                    for a in range(2):
                        last = nc.tensor.matmul(p_g[u % 2][:, a * S:(a + 1) * S], w1_pack[:, q * 128:(q + 1) * 128],
                                                h_pack[:, 2 * pair + a, :], start=True, stop=True)
                    last.then_inc(g_ready, 1)
                    if u > 4 and u % 2 == 1:
                        outputs(b, (u - 5) // 2)
                    if not zero(b):
                        last_products(b - 1, u)
                    if n is not None:
                        front(u, n)

            for u in range(UNITS):
                front(u, 0)
            experts(0, 1)
            with pe.Fori(1, B - 1) as b:
                experts(b, b + 1)
            experts(B - 1, None)
            for u in range(UNITS):
                last_products(B - 1, u)


_INS = ["L0_attn_x", "L0_attn_Wqkv", "L0_attn_Wout", "L0_attn_Wpos", "L0_attn_coeffs", "L0_ffn_Wm", "L0_ffn_bm",
        "L0_ffn_expert_emb", "L0_ffn_W1", "L0_ffn_b1", "L0_ffn_W2", "L0_ffn_b2", "L0_ffn_Wo", "L0_ffn_bo"]


def constants():
    import numpy as np
    ramp = np.linspace(0.0, 1.0, RES).astype(np.float32)
    dist = np.abs(np.arange(1024) - (S - 1)).astype(np.float32) / np.float32(S - 1)
    index = np.clip(np.round(dist * np.float32(RES - 1)).astype(np.int32), 0, RES - 1)
    fir = np.zeros((TAPS, 1024), np.float32)
    for t in range(TAPS):
        at = index - t
        fir[t] = np.where(at >= 0, ramp[np.maximum(at, 0)], 0)
    comb = np.zeros((128, 2, 2, SD), np.float32)
    for p in range(128):
        for k in range(2):
            comb[p, k, k, p % SD] = 1
    rank = np.tile(np.arange(E, 0, -1, dtype=np.float32), (128, 1))
    return {"c_fir": fir, "c_comb": comb.reshape(128, 64), "c_rank": rank}


def kernel(**inputs):
    import numpy as np
    import concourse.bacc as bacc
    from concourse.bass_utils import run_bass_kernel_spmd

    nc = bacc.Bacc("TRN2", target_bir_lowering=False, num_devices=1)
    arrays, args = {}, []
    given = {name: np.ascontiguousarray(inputs[name]) for name in _INS}
    given["L0_attn_Wpos"] = np.ascontiguousarray(given["L0_attn_Wpos"].T)
    given["L0_ffn_b2"] = np.ascontiguousarray(given["L0_ffn_b2"].reshape(2, 8 * SD).T)
    for name, a in {**given, **constants()}.items():
        arrays["in_" + name] = a
        args.append(nc.dram_tensor("in_" + name, a.shape, mybir.dt.from_np(a.dtype), kind="ExternalInput").ap())
    out = nc.dram_tensor("out", (B, S, D), mybir.dt.float32, kind="ExternalOutput").ap()
    layer_kernel(nc, *args, out)
    r = run_bass_kernel_spmd(nc, [arrays], core_ids=[0])
    return r.results[0]["out"]
```
